# Optimizing a Trainium2 kernel written in Bass

```python
import numpy as np
import jax
import jax.numpy as jnp

def _softmax(x, axis=-1):
    return jax.nn.softmax(x, axis=axis)

def _gelu(x):
    return jax.nn.gelu(x, approximate=True)

def _silu(x):
    return jax.nn.silu(x)

def _sigmoid(x):
    return jax.nn.sigmoid(x)

def _layernorm(x, axis=-1, eps=1e-05):
    m = jnp.mean(x, axis=axis, keepdims=True)
    v = jnp.var(x, axis=axis, keepdims=True)
    return (x - m) / jnp.sqrt(v + eps)

def _scatter_add(tgt, idx, src, axis=0):
    return tgt.at[idx].add(src)

def _segment_sum(src, seg, n):
    return jax.ops.segment_sum(src, seg, n)
kernel_name = 'mk_lm_tower_d1_tok_ids2048_r4_0e961c'

def setup_inputs(seed: int=0):
    np.random.seed(seed)
    _w = jnp.asarray

    def _rec_inputs():
        import jax
        import jax.numpy as jnp
        _rk = jax.random.key(seed)
        x = jax.random.randint(jax.random.fold_in(_rk, 1), (2, 1024), 0, 128, jnp.int32)
        return x
    x = _rec_inputs()

    def _L0_tok_setup():
        import jax, jax.numpy as jnp
        import numpy as np
        VOCAB = 128
        D_VIS = 512
        D_TXT = 512
        EPS = 1e-06
        VOCAB_OFFSET = 0

        def rms_norm(x, weight, eps):
            xf = x.astype(jnp.float32)
            var = jnp.mean(xf * xf, axis=-1, keepdims=True)
            normed = xf * jax.lax.rsqrt(var + eps)
            if weight is not None:
                normed = normed * weight.astype(jnp.float32)
            return normed.astype(x.dtype)
        key = jax.random.key(seed)
        k_ids, k_emb, k_w, k_proj = jax.random.split(key, 4)
        input_ids = jax.random.randint(k_ids, (8, 1024), 0, VOCAB, dtype=jnp.int64)
        emb_table = jax.random.normal(k_emb, (VOCAB, D_VIS), dtype=jnp.float32) * 0.02
        norm_weight = jnp.ones((D_VIS,), dtype=jnp.float32) + 0.01 * jax.random.normal(k_w, (D_VIS,), dtype=jnp.float32)
        proj_weight = jax.random.normal(k_proj, (D_TXT, D_VIS), dtype=jnp.float32) * 0.02
        return {'input_ids': input_ids, 'emb_table': emb_table, 'norm_weight': norm_weight, 'proj_weight': proj_weight}
    _L0_tok_all = _L0_tok_setup()
    _L0_tok_in = {k: v for k, v in _L0_tok_all.items() if k in ('emb_table', 'norm_weight', 'proj_weight')}
    del _L0_tok_all

    def _L0_attn_setup():
        import math
        import jax, jax.numpy as jnp
        import numpy as np
        B, T, D = (2, 512, 512)
        NH, NKV = (32, 8)
        HD = D // NH
        key = jax.random.key(seed)
        kx, kq, kk, kv, ko = jax.random.split(key, 5)
        s = 1.0 / math.sqrt(D)
        return {'x': jax.random.normal(kx, (B, T, D), dtype=jnp.float32), 'wq': jax.random.normal(kq, (D, NH * HD), dtype=jnp.float32) * s, 'wk': jax.random.normal(kk, (D, NKV * HD), dtype=jnp.float32) * s, 'wv': jax.random.normal(kv, (D, NKV * HD), dtype=jnp.float32) * s, 'wo': jax.random.normal(ko, (NH * HD, D), dtype=jnp.float32) * s}
    _L0_attn_all = _L0_attn_setup()
    _L0_attn_in = {k: v for k, v in _L0_attn_all.items() if k in ('wq', 'wk', 'wv', 'wo')}
    del _L0_attn_all

    def _L0_ffn_setup():
        import jax, jax.numpy as jnp
        import numpy as np
        DIM_IN = 512
        DIM_HIDDEN = 2048
        key = jax.random.key(seed)
        k_x, k_g, k_u, k_d = jax.random.split(key, 4)
        s_in = 1.0 / np.sqrt(DIM_IN)
        s_hid = 1.0 / np.sqrt(DIM_HIDDEN)
        x = jax.random.normal(k_x, (4, 512, DIM_IN), dtype=jnp.float32)
        w_gate = jax.random.uniform(k_g, (DIM_HIDDEN, DIM_IN), jnp.float32, -s_in, s_in)
        w_up = jax.random.uniform(k_u, (DIM_HIDDEN, DIM_IN), jnp.float32, -s_in, s_in)
        w_down = jax.random.uniform(k_d, (DIM_IN, DIM_HIDDEN), jnp.float32, -s_hid, s_hid)
        return {'x': x, 'w_gate': w_gate, 'w_up': w_up, 'w_down': w_down}
    _L0_ffn_all = _L0_ffn_setup()
    _L0_ffn_in = {k: v for k, v in _L0_ffn_all.items() if k in ('w_gate', 'w_up', 'w_down')}
    del _L0_ffn_all
    return {'x': x, 'L0_tok_emb_table': _L0_tok_in['emb_table'], 'L0_tok_norm_weight': _L0_tok_in['norm_weight'], 'L0_tok_proj_weight': _L0_tok_in['proj_weight'], 'L0_attn_wq': _L0_attn_in['wq'], 'L0_attn_wk': _L0_attn_in['wk'], 'L0_attn_wv': _L0_attn_in['wv'], 'L0_attn_wo': _L0_attn_in['wo'], 'L0_ffn_w_gate': _L0_ffn_in['w_gate'], 'L0_ffn_w_up': _L0_ffn_in['w_up'], 'L0_ffn_w_down': _L0_ffn_in['w_down']}

def reference(x, L0_tok_emb_table, L0_tok_norm_weight, L0_tok_proj_weight, L0_attn_wq, L0_attn_wk, L0_attn_wv, L0_attn_wo, L0_ffn_w_gate, L0_ffn_w_up, L0_ffn_w_down):
    import jax
    import jax.numpy as jnp

    def _L0_tok_ref(input_ids, emb_table, norm_weight, proj_weight):
        import jax, jax.numpy as jnp
        import numpy as np
        VOCAB = 128
        D_VIS = 512
        D_TXT = 512
        EPS = 1e-06
        VOCAB_OFFSET = 0

        def rms_norm(x, weight, eps):
            xf = x.astype(jnp.float32)
            var = jnp.mean(xf * xf, axis=-1, keepdims=True)
            normed = xf * jax.lax.rsqrt(var + eps)
            if weight is not None:
                normed = normed * weight.astype(jnp.float32)
            return normed.astype(x.dtype)
        hard_emb = emb_table[input_ids - VOCAB_OFFSET]
        hard_emb_norm = rms_norm(hard_emb, norm_weight, EPS)
        proj = jnp.einsum('bsd,ed->bse', hard_emb_norm, proj_weight)
        return rms_norm(proj, None, EPS)

    def _L0_attn_ref(x, wq, wk, wv, wo):
        import math
        import jax, jax.numpy as jnp
        import numpy as np
        B, T, D = (2, 512, 512)
        NH, NKV = (32, 8)
        HD = D // NH
        bsz, seqlen, _ = x.shape
        q = (x @ wq).reshape(bsz, seqlen, NH, HD).transpose(0, 2, 1, 3)
        k = (x @ wk).reshape(bsz, seqlen, NKV, HD).transpose(0, 2, 1, 3)
        v = (x @ wv).reshape(bsz, seqlen, NKV, HD).transpose(0, 2, 1, 3)
        rep = NH // NKV
        k = jnp.repeat(k, rep, axis=1)
        v = jnp.repeat(v, rep, axis=1)
        att = jnp.einsum('bhqd,bhkd->bhqk', q.astype(jnp.float32), k.astype(jnp.float32)) / math.sqrt(HD)
        mask = jnp.triu(jnp.ones((seqlen, seqlen), dtype=bool), k=1)
        att = jnp.where(mask[None, None, :, :], -jnp.inf, att)
        att = jax.nn.softmax(att, axis=-1)
        y = jnp.einsum('bhqk,bhkd->bhqd', att, v.astype(jnp.float32)).astype(q.dtype)
        y = y.transpose(0, 2, 1, 3).reshape(bsz, seqlen, NH * HD)
        return y @ wo

    def _L0_ffn_ref(x, w_gate, w_up, w_down):
        import jax, jax.numpy as jnp
        import numpy as np
        DIM_IN = 512
        DIM_HIDDEN = 2048
        gate = jnp.einsum('bsd,hd->bsh', x, w_gate)
        up = jnp.einsum('bsd,hd->bsh', x, w_up)
        gated = jax.nn.silu(gate) * up
        return jnp.einsum('bsh,dh->bsd', gated, w_down)
    h = _L0_tok_ref(x, L0_tok_emb_table, L0_tok_norm_weight, L0_tok_proj_weight)
    h = h + _L0_attn_ref(_layernorm(h, axis=-1), L0_attn_wq, L0_attn_wk, L0_attn_wv, L0_attn_wo)
    h = h + _L0_ffn_ref(_layernorm(h, axis=-1), L0_ffn_w_gate, L0_ffn_w_up, L0_ffn_w_down)
    return h

_drawn_inputs = setup_inputs


def setup_inputs(seed=0):
    import zlib

    import numpy as np

    out = dict(_drawn_inputs(seed))
    spreads = {}
    factors = {}
    for name, (base, spread) in spreads.items():
        noise = np.random.default_rng([zlib.crc32(name.encode()), seed]).standard_normal(out[name].shape)
        drawn = base * np.exp(spread * noise) if base else spread * noise
        out[name] = jnp.asarray(drawn.astype(out[name].dtype))
    for name, factor in factors.items():
        out[name] = (out[name] * factor).astype(out[name].dtype)
    return out
```

```python
import concourse.bass as bass
from concourse import mybir
from contextlib import ExitStack

ALU = mybir.AluOpType
ACT = mybir.ActivationFunctionType
AX = mybir.AxisListType
F32 = mybir.dt.float32
F16 = mybir.dt.float16
BF16 = mybir.dt.bfloat16
I32 = mybir.dt.int32
ABSMAX = bass.bass_isa.ReduceOp.max

P = 128
B, SEQ, VOCAB, D = 2, 1024, 128, 512
HEADS, KV, HD = 32, 8, 16
HID = 2048
TOK = B * SEQ
DC = D // P
HC = HID // P
TILES = TOK // P
BLK = 256
TPB = BLK // P
BLOCKS = TOK // BLK
REP = HEADS // KV
GT = KV
GB = GT * TPB
GW = REP * VOCAB
PVW = 2 * HD + 1
SLOTS = HC + 4 * TPB
H0_SLOT, Y_SLOT, YT_SLOT, WO_SLOT, DEV_SLOT, NORM_SLOT, XN_SLOT = (9, 18), (11, 19), (13, 20), (14, 21), (15, 22), (16, 22), (17, 23)
PIECES = [(w, c, p) for w in range(3) for p in ("scale", "split") for c in range(4)]
RING = 3
EPS_RMS, EPS_LN = 1e-6, 1e-5
NEG = -3.0e38
X_UP = 2.0 ** 11
C_UP = 32.0
TINY = 1e-30
U_MAX, U_RED, U_SPLIT, D_BOUND, D_RED = [0, 1, 2, 3], 4, [5, 6, 7, 8], [9, 10, 11, 12], 14
RSQRT_MAGIC = float(0x5F3759DF - (1 << 22) - (1 << 31))
NEWTON = 3
LN_STEPS = 3 + 2 + 2 * NEWTON


def lm_block(nc, x_row, x_col, emb, nw, projT, wq, wk, wv, wo, wgT, wuT, wdT, out):
    ctx = ExitStack()
    with ctx:
        def sb(name, width, dt):
            return ctx.enter_context(nc.sbuf_tensor(name, [P, width], dt))

        def sem(name):
            return ctx.enter_context(nc.semaphore(name))

        Gs = sb("gate_split", 2 * DC * HID, F16)
        Us = sb("up_split", 2 * DC * HID, F16)
        Ds = sb("down_split", 2 * DC * HID, F16)
        gated = sb("gated_split", 2 * HC * BLK, F16)
        Gh, Gl = (Gs[:, i * DC * HID:(i + 1) * DC * HID].rearrange("p (k h) -> p k h", k=DC) for i in (0, 1))
        Uh, Ul = (Us[:, i * DC * HID:(i + 1) * DC * HID].rearrange("p (k h) -> p k h", k=DC) for i in (0, 1))
        Dh, Dl = (Ds[:, i * HC * D:(i + 1) * HC * D].rearrange("p (j n) -> p j n", j=HC) for i in (0, 1))
        gth, gtl = (gated[:, i * HC * BLK:(i + 1) * HC * BLK].rearrange("p (j n) -> p j n", j=HC) for i in (0, 1))
        Sh = sb("score_hi", HEADS * VOCAB, F16)
        Sl = sb("score_lo", HEADS * VOCAB, F16)
        Wo = sb("wo_split", 2 * DC * D, F16)
        Woh, Wol = (Wo[:, i * DC * D:(i + 1) * DC * D].rearrange("p (c n) -> p c n", c=DC) for i in (0, 1))
        H0 = sb("h0_split", 2 * D, F16)
        Va = sb("v_hi_lo_one", KV * PVW, F16)
        Va3 = Va[:, :].rearrange("p (g c) -> p g c", g=KV)
        OT = sb("onehot_T", TOK, F16)
        Cn = sb("counts", TILES * VOCAB, F16)
        Pen = sb("unseen_penalty", TILES * VOCAB, BF16)
        xT = sb("xn_T_split", 2 * DC * BLK, F16)
        xTh, xTl = (xT[:, i * DC * BLK:(i + 1) * DC * BLK].rearrange("p (c n) -> p c n", c=DC) for i in (0, 1))
        T = [sb(f"weights{i}", GW, F32) for i in range(4)]
        WTh = [sb(f"weights_T_hi{i}", GW, F16) for i in range(2)]
        WTl = [sb(f"weights_T_lo{i}", GW, F16) for i in range(2)]
        PVs = [sb(f"pv{i}", HEADS * PVW, F32) for i in range(2)]
        y = sb("y", D, F32)
        yT = sb("y_T_split", 2 * D, F16)
        h0s = sb("h0_rows", D, F32)
        h1n = [sb(f"h1_next{i}", D, F32) for i in range(2)]
        h1c = [sb(f"h1_cur{i}", D, F32) for i in range(2)]
        xn = sb("xn", D, F32)
        th = [sb(f"tanh{i}", BLK, F32) for i in range(2)]
        ffn = sb("ffn_results", 2 * D + 4 * BLK, F32)
        outs = [ffn[:, i * D:(i + 1) * D] for i in range(2)]
        ag, g2 = ([ffn[:, 2 * D + i * BLK:2 * D + (i + 1) * BLK] for i in (j, j + 1)] for j in (0, 2))
        mx = [sb(f"row_max{i}", REP, F32) for i in range(4)]
        nm = [sb(f"exp_bias{i}", REP, F32) for i in range(4)]
        rden = [sb(f"rden{i}", HEADS, F32) for i in range(2)]
        ident = sb("ident", P, F32)
        st = sb("ln_stats", 16, F32)
        sc = sb("scales", 48, F32)
        pm = sb("part_max", 40, F32)

        u32 = Us[:, :].bitcast(F32)
        d32 = Ds[:, :].bitcast(F32)
        t_KE = u32[:, 0:4096].rearrange("p (m h v) -> p m h v", m=4, h=8)
        t_proj = u32[:, 4096:6144].rearrange("p (k n) -> p k n", k=DC)
        t_wq = u32[:, 6144:8192].rearrange("p (k n) -> p k n", k=DC)
        t_wo = d32[:, 0:2048]
        t_abs = PVs[0][:, 0:1024].bitcast(F16)
        t_emb, t_en, t_sq, t_h0, t_xt = (d32[:, 2048 + 512 * i:2560 + 512 * i] for i in range(5))
        t_eT = d32[:, 4608:5120].rearrange("p (k u) -> p k u", k=DC)
        t_xtT = d32[:, 5120:5632].rearrange("p (k u) -> p k u", k=DC)
        t_qT = d32[:, 5632:6144].rearrange("p (k u) -> p k u", k=DC)
        t_wk = d32[:, 6144:6656].rearrange("p (k n) -> p k n", k=DC)
        t_wv = d32[:, 6656:7168].rearrange("p (k n) -> p k n", k=DC)
        t_wkr = T[0], T[1], T[2], T[3]
        t_on = Gs[:, 0:2048].bitcast(BF16)
        t_xb = Gs[:, 2048:6144].bitcast(I32)
        g32 = Gs[:, 6144:].bitcast(F32)
        t_iota_r, t_iota_c, t_xc, t_nw, t_mask = (g32[:, 0:128], g32[:, 128:129], g32[:, 132:148],
                                                  g32[:, 148:152], g32[:, 152:160])
        t_xci = g32[:, 160:176].bitcast(I32)
        t_tri, t_ones = (g32[:, 192 + 64 * i:256 + 64 * i].bitcast(BF16) for i in (0, 1))
        stage = [gated[:, 0:4096].bitcast(F32), gated[:, 4096:8192].bitcast(F32), ffn[:, 0:HID]]

        bank = [ctx.enter_context(nc.psum_tensor(f"bank{i}", [P, 512], F32)) for i in range(8)]
        b_S, b_tail, b_WT, b_PV = bank[:4]
        b_ffn = bank[4:]

        x_in, emb_in, proj_in, qkv_in, wo_in = (sem(n) for n in ("x_in", "emb_in", "proj_in", "qkv_in", "wo_in"))
        stage_in = [sem(f"stage{i}_in") for i in range(RING)]
        stage_used = [sem(f"stage{i}_used") for i in range(RING)]
        consts = sem("consts")
        passed = sem("waits_passed")
        cstep = sem("const_step")
        vstep, astep = sem("vector_step"), sem("scalar_step")
        onehot = sem("onehot")
        cnt_up = sem("counts_scaled")
        cnt_mm, cnt_ev = sem("counts_mm"), sem("counts_evacuated")
        tab = {n: sem("tab_" + n) for n in ("ssq1", "en", "eT_mm", "eT", "proj", "ssq2", "h0", "h0hi", "xt", "xtT_mm", "xtT",
                                            "wkr", "q_mm", "k_mm", "v_mm", "q", "ke", "s_mm", "maxes", "reduced",
                                            "vwo", "scaled", "hi", "lo", "vone", "fmax")}
        split_hi, split_lo = ([sem(f"{w}_{half}") for w in ("gate", "up", "down")] for half in ("hi", "lo"))
        red = [sem(f"{w}_reduced") for w in ("gate", "up", "down")]
        bound = [sem(f"{w}_bound") for w in ("gate", "up", "down")]
        scaled = [sem(f"{w}_scaled") for w in ("gate", "up", "down")]
        scores = sem("scores_ready")
        t_added, max_done, bias_rdy = sem("t_added"), sem("max_done"), sem("bias_ready")
        exp_done, w_rdy = sem("exp_done"), sem("w_ready")
        wt_rdy, wt_hi, wt_lo = sem("wt_ready"), sem("wt_hi"), sem("wt_lo")
        pv_rdy, pv_ev = sem("pv_ready"), sem("pv_evacuated")
        h0_rdy, h0_ev = sem("h0_ready"), sem("h0_evacuated")
        rd_rdy, num_rdy, y_rdy = sem("rden_ready"), sem("num_ready"), sem("y_ready")
        yt_rdy, yt_hi, yt_lo = sem("yT_ready"), sem("yT_hi"), sem("yT_lo")
        wo_rdy, h1_rdy, lnstep, xn_rdy = sem("wo_ready"), sem("h1_ready"), sem("ln_step"), sem("xn_ready")
        xt_rdy, xt_hi, xt_lo = sem("xT_ready"), sem("xT_hi"), sem("xT_lo")
        gu_rdy, th_rdy, a_rdy, g2_rdy = sem("gu_ready"), sem("tanh_ready"), sem("act_gate_ready"), sem("gated_ready")
        gt_hi, gt_lo = sem("gated_hi"), sem("gated_lo")
        dn_rdy, fin_rdy, h1_cp = sem("down_ready"), sem("out_ready"), sem("h1_copied")
        stored = [sem("stored0"), sem("stored1")]

        POW = dict(S=0, V=1, wo=2, g=3, u=4, d=5)

        def pw(n):
            return sc[:, POW[n]:POW[n] + 1]

        def col(i):
            return sc[:, i:i + 1]

        s_S, s_V, s_wo, s_g, s_u, s_d = (col(8 + i) for i in range(6))
        c_exp, c_nexp, c_vo, c_tanh, c_out, c_tmp = (col(16 + i) for i in range(6))

        def grp(ap):
            return ap.rearrange("p (h v) -> p h v", h=REP)

        def piece_src(i):
            w, c, _ = PIECES[i]
            if w < 2:
                return (wgT, wuT)[w][c * P:(c + 1) * P, :]
            return wdT.rearrange("(j p) n -> p j n", p=P)[:, 4 * c:4 * c + 4, :]

        def piece_dst(i, half):
            w, c, _ = PIECES[i]
            at = half * DC * HID + c * HID
            return (Gs, Us, Ds)[w][:, at:at + HID]

        def wait_apart(eng, signal, value):
            eng.wait_ge(signal, value)
            eng.sem_inc(passed, 1)

        def arrived(eng, i):
            eng.wait_ge(stage_in[i % RING], 16 * (i // RING + 1))

        def piece(w, purpose, c):
            return PIECES.index((w, c, purpose))

        block = ctx.enter_context(nc.Block())

        @block.sync
        def _(sp):
            sp.sem_inc(fin_rdy, TPB)
            for k in range(TPB):
                sp.sem_inc(stored[k], 16)
            sp.dma_start(t_xci, x_col).then_inc(x_in, 16)
            sp.dma_start(t_xb, x_row.partition_broadcast(P)).then_inc(x_in, 16)
            sp.dma_start(t_emb, emb).then_inc(emb_in, 16)
            sp.dma_start(t_nw, nw).then_inc(emb_in, 16)
            sp.dma_start(t_proj, projT.rearrange("(k p) n -> p k n", p=P)).then_inc(proj_in, 16)
            sp.dma_start(t_wk, wk.rearrange("(k p) n -> p k n", p=P)).then_inc(qkv_in, 16)
            sp.dma_start(t_wq, wq.rearrange("(k p) n -> p k n", p=P)).then_inc(qkv_in, 16)
            sp.dma_start(t_wv, wv.rearrange("(k p) n -> p k n", p=P)).then_inc(qkv_in, 16)
            sp.dma_start(t_wo.rearrange("p (k n) -> p k n", k=DC),
                         wo.rearrange("(k p) n -> p k n", p=P)).then_inc(wo_in, 16)
            for i, (w, _, _) in enumerate(PIECES):
                if i >= RING:
                    sp.wait_ge(stage_used[i % RING], i // RING)
                dst = stage[i % RING]
                if w == 2:
                    dst = dst.rearrange("p (j n) -> p j n", j=4)
                sp.dma_start(dst, piece_src(i)).then_inc(stage_in[i % RING], 16)
            with sp.Fori(0, BLOCKS) as m:
                for k in range(TPB):
                    sp.wait_ge(fin_rdy, m * TPB + TPB + k + 1)
                    sp.dma_start(out[bass.ds(m * BLK + k * P, P), :], outs[k][:, :]).then_inc(stored[k], 16)
            for k in range(TPB):
                sp.wait_ge(stored[k], 16 * BLOCKS + 16)

        @block.gpsimd
        def _(pool):
            g = nc.gpsimd
            g.memset(ident[:, :], 0.0).then_inc(cstep, 1)
            g.memset(t_tri, 1.0).then_inc(cstep, 1)
            g.memset(t_ones, 1.0)
            g.memset(t_mask, 1.0).then_inc(cstep, 1)
            g.memset(Va3[:, :, 2 * HD:PVW], 1.0).then_inc(tab["vone"], 1)
            g.iota(t_iota_r, [[1, P]], base=0, channel_multiplier=0, allow_small_or_imprecise_dtypes=True)
            g.iota(t_iota_c, [[1, 1]], base=0, channel_multiplier=1, allow_small_or_imprecise_dtypes=True)
            pool.wait_ge(cstep, 3)
            g.affine_select(out=ident[:, :], in_=ident[:, :], compare_op=ALU.not_equal, fill=1.0, base=0,
                            pattern=[[-1, P]], channel_multiplier=1)
            g.affine_select(out=t_tri, in_=t_tri, compare_op=ALU.is_ge, fill=0.0, base=0,
                            pattern=[[1, P]], channel_multiplier=-1)
            g.affine_select(out=t_mask, in_=t_mask, compare_op=ALU.is_ge, fill=0.0, base=0,
                            pattern=[[-HD, 8]], channel_multiplier=1).then_inc(cstep, 1)
            pool.wait_ge(cstep, 4)
            g.affine_select(out=t_mask, in_=t_mask, compare_op=ALU.is_ge, fill=0.0, base=HD - 1,
                            pattern=[[HD, 8]], channel_multiplier=-1).then_inc(consts, 1)
            pool.wait_ge(qkv_in, 48)
            for k in range(DC):
                last = g.tensor_copy(t_wkr[k][:, :].rearrange("p (g r d) -> p g r d", g=KV, r=REP),
                                     t_wk[:, k, :].rearrange("p (g d) -> p g d", g=KV).unsqueeze(2)
                                     .broadcast_to([P, KV, REP, HD]))
            last.then_inc(tab["wkr"], 1)
            pool.wait_ge(tab["maxes"], 1)
            g.partition_all_reduce(pm[:, 16:20], pm[:, 0:4], P, ABSMAX).then_inc(tab["reduced"], 1)

            def reduce_bound(w):
                pool.wait_ge(bound[w], 4 if w == 2 else 1)
                if w == 2:
                    g.partition_all_reduce(pm[:, 24:28], pm[:, 4:8], P, ABSMAX).then_inc(red[w], 1)
                else:
                    g.partition_all_reduce(pm[:, 20:21], pm[:, 12:13], P, ABSMAX).then_inc(red[w], 1)

            def prep(s):
                if s == U_RED:
                    reduce_bound(1)
                if s == D_RED:
                    reduce_bound(2)

            def slots(n, att, ffn, m):
                if ffn:
                    pool.wait_ge(fin_rdy, m * TPB + TPB)
                    wait_apart(pool, h1_rdy, m * TPB + TPB)
                    g.tensor_copy(h1c[0][:, :], h1n[0][:, :])
                    g.tensor_copy(h1c[1][:, :], h1n[1][:, :]).then_inc(h1_cp, 1)
                for s in range(SLOTS):
                    if att and s < GB:
                        k = s // GT
                        wait_apart(pool, exp_done, n * GB + s + 1)
                        w = grp(T[s % 4][:, :])
                        cs = Cn[:, bass.ds(n * BLK + k * P, P)].unsqueeze(1).broadcast_to([P, REP, VOCAB])
                        g.tensor_tensor(w, w, cs, ALU.mult).then_inc(w_rdy, 1)
                    if ffn and 1 <= s <= HC:
                        j = s - 1
                        pool.wait_ge(gt_hi, m * HC + j + 1)
                        g.tensor_tensor(gtl[:, j, :], g2[j % 2][:, :], gth[:, j, :], ALU.subtract).then_inc(gt_lo, 1)
                    for k in range(TPB):
                        if att and s == Y_SLOT[k]:
                            pool.wait_ge(pv_ev, n * GB + GT * k + GT)
                            if not isinstance(n, int) or n * TPB + k > 0:
                                pool.wait_ge(yt_rdy, n * TPB + k)
                            pv = PVs[k][:, :].rearrange("p (h c) -> p h c", h=HEADS)
                            yv = y[:, :].rearrange("p (h d) -> p h d", h=HEADS)
                            g.tensor_tensor(yv, pv[:, :, 0:HD], pv[:, :, HD:2 * HD], ALU.add).then_inc(num_rdy, 1)
                            pool.wait_ge(num_rdy, n * TPB + k + 1)
                            pool.wait_ge(rd_rdy, n * TPB + k + 1)
                            g.tensor_tensor(yv, yv, rden[k][:, :].unsqueeze(2).broadcast_to([P, HEADS, HD]),
                                            ALU.mult).then_inc(y_rdy, 1)
                    if not ffn:
                        prep(s)

            slots(0, True, False, 0)
            with pool.Fori(1, BLOCKS) as n:
                slots(n, True, True, n - 1)
            slots(0, False, True, BLOCKS - 1)

        @block.scalar
        def _(act):
            a = nc.scalar
            act.wait_ge(emb_in, 32)
            a.activation(t_sq, t_emb, ACT.Square, accum_out=st[:, 0:1]).then_inc(tab["ssq1"], 1)
            for i in range(4):
                act.wait_ge(cnt_mm, i + 1)
                a.activation(Cn[:, i * 512:(i + 1) * 512], bank[i][:, :], ACT.Copy, scale=C_UP).then_inc(cnt_up, 1)
            act.wait_ge(tab["proj"], 1)
            act.wait_ge(tab["ssq1"], 1)
            a.activation(t_sq, bank[5][:, :], ACT.Square, accum_out=st[:, 1:2]).then_inc(tab["ssq2"], 1)
            act.wait_ge(tab["h0"], 1)
            a.activation(H0[:, 0:D], t_h0, ACT.Copy, scale=X_UP).then_inc(tab["h0hi"], 1)
            act.wait_ge(wo_in, 16)
            a.activation(t_abs, t_wo, ACT.Abs,
                         accum_out=pm[:, 2:3]).then_inc(tab["fmax"], 1)
            act.wait_ge(tab["xtT_mm"], 1)
            a.activation(t_xtT.rearrange("p k u -> p (k u)"), bank[4][:, :], ACT.Copy).then_inc(tab["xtT"], 1)
            act.wait_ge(tab["q_mm"], 1)
            a.activation(t_qT.rearrange("p k u -> p (k u)"), bank[6][:, :], ACT.Copy).then_inc(tab["q"], 1)
            act.wait_ge(tab["scaled"], 1)
            for i in range(8):
                a.activation(Sh[:, i * 512:(i + 1) * 512], bank[i][:, :], ACT.Copy, scale=s_S).then_inc(tab["hi"], 1)
            vs = xn[:, 0:P].rearrange("p (g d) -> p g d", g=KV)
            a.activation(Va3[:, :, 0:HD], vs, ACT.Copy, scale=s_V).then_inc(tab["hi"], 1)
            a.activation(Wo[:, 0:DC * D], t_wo, ACT.Copy, scale=s_wo).then_inc(tab["hi"], 1)

            def split_high(w, c):
                i = piece(w, "split", c)
                arrived(act, i)
                if c == 0 and w:
                    act.wait_ge(scaled[w], 1)
                a.activation(piece_dst(i, 0), stage[i % RING], ACT.Copy,
                             scale=(s_g, s_u, s_d)[w]).then_inc(split_hi[w], 1)

            def prep(s):
                if s in U_SPLIT:
                    split_high(1, U_SPLIT.index(s))
                if s in D_BOUND:
                    c = D_BOUND.index(s)
                    i = piece(2, "scale", c)
                    arrived(act, i)
                    a.activation(stage[i % RING], stage[i % RING], ACT.Abs,
                                 accum_out=pm[:, 4 + c:5 + c]).then_inc(bound[2], 1)
                    act.wait_ge(bound[2], c + 1)
                    act.sem_inc(stage_used[i % RING], 1)

            for c in range(4):
                split_high(0, c)

            def slots(n, att, ffn, m):
                for s in range(SLOTS):
                    if ffn and 1 <= s <= HC:
                        j = s - 1
                        act.wait_ge(gu_rdy, m * HC + j + 1)
                        if j > 1:
                            act.wait_ge(a_rdy, m * HC + j - 1)
                        a.activation(th[j % 2][:, :], b_ffn[j % 4][:, 0:BLK], ACT.Tanh, scale=c_tanh).then_inc(th_rdy, 1)
                    if att and 2 <= s < GB + 2:
                        q = s - 2
                        act.wait_ge(wt_rdy, n * GB + q + 1)
                        if not isinstance(n, int) or n * GB + q - 1 > 0:
                            act.wait_ge(pv_rdy, n * GB + q - 1)
                        a.activation(WTh[q % 2][:, :], b_WT[:, :], ACT.Copy).then_inc(wt_hi, 1)
                    if att and s < GB:
                        act.wait_ge(bias_rdy, n * GB + s + 1)
                        for h in range(REP):
                            t = T[s % 4][:, h * VOCAB:(h + 1) * VOCAB]
                            last = a.activation(t, t, ACT.Exp, bias=nm[s % 4][:, h:h + 1], scale=c_exp)
                        last.then_inc(exp_done, 1)
                    if att and 3 <= s < GB + 3:
                        k, hg = divmod(s - 3, GT)
                        act.wait_ge(pv_rdy, n * GB + s - 2)
                        if hg == 0 and (not isinstance(n, int) or n * TPB + k - 1 > 0):
                            act.wait_ge(y_rdy, n * TPB + k - 1)
                        w = REP * PVW
                        a.activation(PVs[k][:, hg * w:(hg + 1) * w], b_PV[:, 0:w], ACT.Copy).then_inc(pv_ev, 1)
                    if ffn and 1 <= s <= HC:
                        j = s - 1
                        act.wait_ge(g2_rdy, m * HC + j + 1)
                        a.activation(gth[:, j, :], g2[j % 2][:, :], ACT.Copy).then_inc(gt_hi, 1)
                    for k in range(TPB):
                        if att and s == H0_SLOT[k]:
                            act.wait_ge(h0_rdy, n * TPB + k + 1)
                            if not isinstance(n, int) or n * TPB + k > 0:
                                act.wait_ge(h1_rdy, n * TPB + k)
                            a.activation(h0s[:, :], b_tail[:, :], ACT.Copy, scale=1.0 / X_UP).then_inc(h0_ev, 1)
                        if att and s == YT_SLOT[k]:
                            act.wait_ge(yt_rdy, n * TPB + k + 1)
                            if not isinstance(n, int) or n * TPB + k > 0:
                                act.wait_ge(wo_rdy, n * TPB + k)
                            a.activation(yT[:, 0:D], b_tail[:, :], ACT.Copy).then_inc(yt_hi, 1)
                        if att and s == XN_SLOT[k]:
                            act.wait_ge(xt_rdy, n * TPB + k + 1)
                            if ffn:
                                act.wait_ge(gu_rdy, m * HC + HC)
                            a.activation(xTh[:, :, k * P:(k + 1) * P],
                                         b_tail[:, :].rearrange("p (c n) -> p c n", c=DC),
                                         ACT.Copy, scale=X_UP).then_inc(xt_hi, 1)
                    if not ffn:
                        prep(s)

            slots(0, True, False, 0)
            for c in range(4):
                split_high(2, c)
            with act.Fori(1, BLOCKS) as n:
                slots(n, True, True, n - 1)
            slots(0, False, True, BLOCKS - 1)

        @block.vector
        def _(dve):
            v = nc.vector
            steps = [0]

            def link(ins):
                steps[0] += 1
                ins.then_inc(vstep, 1)
                dve.wait_ge(vstep, steps[0])

            def rsqrt(half, y0, tmp, chain):
                chain(v.tensor_scalar(tmp.bitcast(I32), half.bitcast(I32), 1, None, ALU.logical_shift_right))
                chain(v.tensor_scalar(y0.bitcast(I32), tmp.bitcast(I32), -1.0, RSQRT_MAGIC, ALU.mult, ALU.add))
                for _ in range(NEWTON):
                    chain(v.scalar_tensor_tensor(tmp, y0, y0, half, ALU.mult, ALU.mult))
                    chain(v.scalar_tensor_tensor(y0, tmp, 1.5, y0, ALU.subtract, ALU.mult))

            dve.wait_ge(x_in, 32)
            dve.wait_ge(consts, 1)
            link(v.tensor_copy(t_xc, t_xci))
            v.tensor_tensor(t_on.rearrange("p (t u) -> p t u", t=TILES),
                            t_iota_r.unsqueeze(1).broadcast_to([P, TILES, VOCAB]),
                            t_xc.unsqueeze(2).broadcast_to([P, TILES, VOCAB]), ALU.is_equal).then_inc(onehot, 1)
            v.tensor_scalar(OT[:, :], t_xb, t_iota_c, None, ALU.is_equal).then_inc(onehot, 1)
            dve.wait_ge(tab["ssq1"], 1)
            link(v.tensor_scalar(st[:, 2:3], st[:, 0:1], 0.5 / D, 0.5 * EPS_RMS, ALU.mult, ALU.add))
            rsqrt(st[:, 2:3], st[:, 3:4], st[:, 13:14], link)
            v.tensor_scalar(t_en, t_emb, st[:, 3:4], None, ALU.mult).then_inc(tab["en"], 1)
            dve.wait_ge(tab["eT_mm"], 1)
            v.tensor_tensor(t_eT, bank[4][:, :].rearrange("p (k u) -> p k u", k=DC),
                            t_nw.unsqueeze(2).broadcast_to([P, DC, VOCAB]), ALU.mult).then_inc(tab["eT"], 1)
            for i in range(4):
                dve.wait_ge(cnt_up, i + 1)
                v.tensor_scalar(Pen[:, i * 512:(i + 1) * 512], bank[i][:, :], 0.0, NEG, ALU.is_equal,
                                ALU.mult).then_inc(cnt_ev, 1)
            dve.wait_ge(tab["ssq2"], 1)
            link(v.tensor_scalar(st[:, 2:3], st[:, 1:2], 0.5 / D, 0.5 * EPS_RMS, ALU.mult, ALU.add))
            rsqrt(st[:, 2:3], st[:, 3:4], st[:, 13:14], link)
            v.tensor_scalar(t_h0, bank[5][:, :], st[:, 3:4], None, ALU.mult).then_inc(tab["h0"], 1)
            dve.wait_ge(tab["h0"], 1)
            link(v.bn_stats(st[:, 4:10], t_h0))
            link(v.bn_aggr(st[:, 10:12], st[:, 4:10]))
            link(v.tensor_scalar(st[:, 2:3], st[:, 11:12], 0.5, 0.5 * EPS_LN, ALU.mult, ALU.add))
            rsqrt(st[:, 2:3], st[:, 12:13], st[:, 13:14], link)
            v.tensor_scalar(t_xt, t_h0, st[:, 10:11], st[:, 12:13], ALU.subtract, ALU.mult).then_inc(tab["xt"], 1)
            dve.wait_ge(tab["h0hi"], 1)
            v.scalar_tensor_tensor(H0[:, D:2 * D], t_h0, X_UP, H0[:, 0:D], ALU.mult,
                                   ALU.subtract).then_inc(tab["lo"], 1)

            def largest(w, c):
                i = piece(w, "scale", c)
                arrived(dve, i)
                v.tensor_reduce(pm[:, 8 + c:9 + c] if w else sc[:, 36 + c:37 + c], stage[i % RING], AX.X, ALU.max,
                                apply_absolute_value=True).then_inc(stage_used[i % RING], 1)

            for c in range(3):
                largest(0, c)
            dve.wait_ge(tab["k_mm"], 1)
            for m in range(DC):
                last = v.tensor_tensor(t_KE[:, m, :, :],
                                       bank[7][:, m * P:(m + 1) * P].unsqueeze(1).broadcast_to([P, 8, VOCAB]),
                                       t_mask.unsqueeze(2).broadcast_to([P, 8, VOCAB]), ALU.mult)
            last.then_inc(tab["ke"], 1)
            dve.wait_ge(tab["v_mm"], 1)
            v.tensor_copy(xn[:, 0:P], bank[5][:, 0:P]).then_inc(tab["vwo"], 1)
            dve.wait_ge(tab["vwo"], 1)
            v.tensor_reduce(pm[:, 1:2], xn[:, 0:P], AX.X, ALU.max, apply_absolute_value=True)
            largest(0, 3)
            dve.wait_ge(stage_used[piece(0, "scale", 3) % RING], piece(0, "scale", 3) // RING + 1)
            v.tensor_reduce(pm[:, 3:4], sc[:, 36:40], AX.X, ALU.max)
            for i in range(8):
                dve.wait_ge(tab["s_mm"], i + 1)
                last = v.tensor_reduce(pm[:, 28 + i:29 + i], bank[i][:, :], AX.X, ALU.max, apply_absolute_value=True)
            link(last)
            dve.wait_ge(tab["fmax"], 1)
            v.tensor_reduce(pm[:, 0:1], pm[:, 28:36], AX.X, ALU.max).then_inc(tab["maxes"], 1)

            def powers(at, n, done):
                link(v.tensor_scalar(sc[:, 24 + at:24 + at + n], pm[:, 16 + at:16 + at + n], TINY, None, ALU.max))
                link(v.tensor_scalar(sc[:, at:at + n].bitcast(I32), sc[:, 24 + at:24 + at + n].bitcast(I32),
                                     0x7F800000, None, ALU.bitwise_and))
                link(v.reciprocal(sc[:, 32 + at:32 + at + n], sc[:, at:at + n]))
                link(v.tensor_scalar(sc[:, 8 + at:8 + at + n], sc[:, 32 + at:32 + at + n], 2.0 ** 14, None, ALU.mult))

            dve.wait_ge(tab["reduced"], 1)
            powers(0, 4, None)
            v.tensor_scalar(c_tanh, pw("g"), 2.0 ** -26, None, ALU.mult)
            v.tensor_scalar(c_exp, pw("S"), 2.0 ** -14 * HD ** -0.5, None, ALU.mult)
            v.tensor_scalar(c_nexp, pw("S"), -(2.0 ** -14) * HD ** -0.5, None, ALU.mult)
            v.tensor_scalar(c_vo, pw("V"), pw("wo"), 2.0 ** -28, ALU.mult, ALU.mult).then_inc(tab["scaled"], 1)
            dve.wait_ge(tab["scaled"], 1)
            for i in range(8):
                dve.wait_ge(tab["hi"], i + 1)
                v.scalar_tensor_tensor(Sl[:, i * 512:(i + 1) * 512], bank[i][:, :], s_S,
                                       Sh[:, i * 512:(i + 1) * 512], ALU.mult, ALU.subtract)
            dve.wait_ge(tab["hi"], 9)
            v.scalar_tensor_tensor(Va3[:, :, HD:2 * HD], xn[:, 0:P].rearrange("p (g d) -> p g d", g=KV), s_V,
                                   Va3[:, :, 0:HD], ALU.mult, ALU.subtract)
            dve.wait_ge(tab["hi"], 10)
            v.scalar_tensor_tensor(Wo[:, DC * D:2 * DC * D], t_wo, s_wo, Wo[:, 0:DC * D], ALU.mult,
                                   ALU.subtract).then_inc(tab["lo"], 1)

            def split_low(w, c):
                i = piece(w, "split", c)
                dve.wait_ge(split_hi[w], c + 1)
                v.scalar_tensor_tensor(piece_dst(i, 1), stage[i % RING], (s_g, s_u, s_d)[w], piece_dst(i, 0),
                                       ALU.mult, ALU.subtract).then_inc(stage_used[i % RING], 1)

            def prep(s):
                if s in U_MAX:
                    largest(1, U_MAX.index(s))
                if s == U_MAX[-1]:
                    i = piece(1, "scale", 3)
                    dve.wait_ge(stage_used[i % RING], i // RING + 1)
                    v.tensor_reduce(pm[:, 12:13], pm[:, 8:12], AX.X, ALU.max).then_inc(bound[1], 1)
                if s == U_RED:
                    dve.wait_ge(red[1], 1)
                    powers(4, 1, None)
                    v.tensor_scalar(c_tmp, pw("g"), pw("u"), None, ALU.mult).then_inc(scaled[1], 1)
                if s in U_SPLIT:
                    split_low(1, U_SPLIT.index(s))
                if s == D_RED:
                    dve.wait_ge(red[2], 1)
                    link(v.tensor_reduce(pm[:, 21:22], pm[:, 24:28], AX.X, ALU.max))
                    powers(5, 1, None)
                    v.tensor_scalar(c_out, c_tmp, pw("d"), 2.0 ** -9, ALU.mult, ALU.mult).then_inc(scaled[2], 1)

            for c in range(4):
                split_low(0, c)

            def slots(n, att, ffn, m):
                done = [0] * TPB
                for s in range(SLOTS):
                    if att and s < GB:
                        k = s // GT
                        dve.wait_ge(scores, n * GB + s + 1)
                        if not isinstance(n, int) or n * GB + s - 3 > 0:
                            dve.wait_ge(wt_rdy, n * GB + s - 3)
                        pen = Pen[:, bass.ds(n * BLK + k * P, P)].unsqueeze(1).broadcast_to([P, REP, VOCAB])
                        v.tensor_tensor(grp(T[s % 4][:, :]), grp(b_S[:, :]), pen, ALU.add).then_inc(t_added, 1)
                        dve.wait_ge(t_added, n * GB + s + 1)
                        v.tensor_reduce(mx[s % 4][:, :], grp(T[s % 4][:, :]), AX.X, ALU.max).then_inc(max_done, 1)
                        dve.wait_ge(max_done, n * GB + s + 1)
                        v.tensor_scalar(nm[s % 4][:, :], mx[s % 4][:, :], c_nexp, None, ALU.mult).then_inc(bias_rdy, 1)
                    if ffn and 1 <= s <= HC:
                        j = s - 1
                        pb = b_ffn[j % 4]
                        dve.wait_ge(th_rdy, m * HC + j + 1)
                        v.scalar_tensor_tensor(ag[j % 2][:, :], th[j % 2][:, :], 1.0, pb[:, 0:BLK], ALU.add,
                                               ALU.mult).then_inc(a_rdy, 1)
                        dve.wait_ge(a_rdy, m * HC + j + 1)
                        if j > 1:
                            dve.wait_ge(gt_lo, m * HC + j - 1)
                        v.scalar_tensor_tensor(g2[j % 2][:, :], pb[:, BLK:2 * BLK], 2.0 ** -56, ag[j % 2][:, :],
                                               ALU.mult, ALU.mult).then_inc(g2_rdy, 1)
                    if att and 2 <= s < GB + 2:
                        q = s - 2
                        dve.wait_ge(wt_hi, n * GB + q + 1)
                        if not isinstance(n, int) or n * GB + q - 1 > 0:
                            dve.wait_ge(pv_rdy, n * GB + q - 1)
                        v.tensor_tensor(WTl[q % 2][:, :], b_WT[:, :], WTh[q % 2][:, :], ALU.subtract).then_inc(wt_lo, 1)
                    for k in range(TPB):
                        def ln_link(ins, k=k):
                            done[k] += 1
                            ins.then_inc(lnstep, 1)
                            dve.wait_ge(lnstep, (n * TPB + k) * LN_STEPS + done[k])

                        if att and s == Y_SLOT[k]:
                            dve.wait_ge(pv_ev, n * GB + GT * k + GT)
                            if not isinstance(n, int) or n * TPB + k - 1 > 0:
                                dve.wait_ge(y_rdy, n * TPB + k - 1)
                            v.reciprocal(rden[k][:, :], PVs[k][:, :].rearrange("p (h c) -> p h c", h=HEADS)[:, :, 2 * HD])\
                                .then_inc(rd_rdy, 1)
                        if att and s == YT_SLOT[k]:
                            dve.wait_ge(yt_hi, n * TPB + k + 1)
                            if not isinstance(n, int) or n * TPB + k > 0:
                                dve.wait_ge(wo_rdy, n * TPB + k)
                            v.tensor_tensor(yT[:, D:2 * D], b_tail[:, :], yT[:, 0:D], ALU.subtract).then_inc(yt_lo, 1)
                        if att and s == WO_SLOT[k]:
                            t = n * TPB + k
                            dve.wait_ge(wo_rdy, t + 1)
                            dve.wait_ge(h0_ev, t + 1)
                            if ffn:
                                dve.wait_ge(h1_cp, m + 1)
                            v.scalar_tensor_tensor(h1n[k][:, :], b_tail[:, :], c_vo, h0s[:, :], ALU.mult,
                                                   ALU.add).then_inc(h1_rdy, 1)
                            dve.wait_ge(h1_rdy, t + 1)
                            done[k] = 0
                            v.bn_stats(st[:, 4:10], h1n[k][:, :]).then_inc(lnstep, 1)
                            done[k] += 1
                            wait_apart(dve, lnstep, t * LN_STEPS + 1)
                            ln_link(v.bn_aggr(st[:, 10:12], st[:, 4:10]))
                            ln_link(v.tensor_scalar(st[:, 2:3], st[:, 11:12], 0.5, 0.5 * EPS_LN, ALU.mult, ALU.add))
                        if att and s == DEV_SLOT[k]:
                            rsqrt(st[:, 2:3], st[:, 12:13], st[:, 13:14], ln_link)
                        if att and s == NORM_SLOT[k]:
                            t = n * TPB + k
                            if not isinstance(n, int) or n * TPB + k > 0:
                                dve.wait_ge(xt_rdy, t)
                            v.tensor_scalar(xn[:, :], h1n[k][:, :], st[:, 10:11], st[:, 12:13], ALU.subtract,
                                            ALU.mult).then_inc(xn_rdy, 1)
                        if att and s == XN_SLOT[k]:
                            dve.wait_ge(xt_hi, n * TPB + k + 1)
                            v.scalar_tensor_tensor(xTl[:, :, k * P:(k + 1) * P],
                                                   b_tail[:, :].rearrange("p (c n) -> p c n", c=DC), X_UP,
                                                   xTh[:, :, k * P:(k + 1) * P], ALU.mult, ALU.subtract).then_inc(xt_lo, 1)
                    for k in range(TPB):
                        if ffn and s == HC + 4 * (k + 1) - (k == TPB - 1):
                            dve.wait_ge(dn_rdy, m * TPB + k + 1)
                            dve.wait_ge(stored[k], m * 16 + 16)
                            v.scalar_tensor_tensor(outs[k][:, :], b_ffn[k][:, :], c_out, h1c[k][:, :], ALU.mult,
                                                   ALU.add).then_inc(fin_rdy, 1)
                    if not ffn:
                        prep(s)

            slots(0, True, False, 0)
            for c in range(4):
                split_low(2, c)
            with dve.Fori(1, BLOCKS) as n:
                slots(n, True, True, n - 1)
            slots(0, False, True, BLOCKS - 1)

        @block.tensor
        def _(pe):
            t = nc.tensor
            on = t_on.rearrange("p (t u) -> p t u", t=TILES)
            pe.wait_ge(onehot, 1)
            per = SEQ // P
            for tl in range(TILES):
                first = tl // per * per
                o = bank[tl // 4][:, (tl % 4) * P:(tl % 4 + 1) * P]
                last = t.matmul(o, t_tri, on[:, tl, :], start=True, stop=tl == first)
                for e in range(first, tl):
                    last = t.matmul(o, t_ones, on[:, e, :], start=False, stop=e == tl - 1)
                if tl % 4 == 3:
                    last.then_inc(cnt_mm, 1)
            pe.wait_ge(tab["en"], 1)
            for k in range(DC):
                last = t.transpose(bank[4][:, k * P:(k + 1) * P], t_en[:, k * P:(k + 1) * P], ident[:, :])
            last.then_inc(tab["eT_mm"], 1)
            pe.wait_ge(tab["eT"], 1)
            pe.wait_ge(proj_in, 16)
            for k in range(DC):
                last = t.matmul(bank[5][:, :], t_eT[:, k, :], t_proj[:, k, :], start=k == 0, stop=k == DC - 1)
            last.then_inc(tab["proj"], 1)
            pe.wait_ge(tab["xt"], 1)
            for k in range(DC):
                last = t.transpose(bank[4][:, k * P:(k + 1) * P], t_xt[:, k * P:(k + 1) * P], ident[:, :])
            last.then_inc(tab["xtT_mm"], 1)
            pe.wait_ge(tab["xtT"], 1)
            pe.wait_ge(tab["wkr"], 1)
            for m in range(DC):
                for k in range(DC):
                    last = t.matmul(bank[7][:, m * P:(m + 1) * P], t_wkr[k][:, m * P:(m + 1) * P], t_xtT[:, k, :],
                                    start=k == 0, stop=k == DC - 1)
            last.then_inc(tab["k_mm"], 1)
            for m in range(DC):
                for k in range(DC):
                    last = t.matmul(bank[6][:, m * P:(m + 1) * P], t_wq[:, k, m * P:(m + 1) * P], t_xtT[:, k, :],
                                    start=k == 0, stop=k == DC - 1)
            last.then_inc(tab["q_mm"], 1)
            for k in range(DC):
                last = t.matmul(bank[5][:, 0:P], t_xtT[:, k, :], t_wv[:, k, :], start=k == 0, stop=k == DC - 1)
            last.then_inc(tab["v_mm"], 1)
            pe.wait_ge(cnt_ev, 4)
            pe.wait_ge(tab["q"], 1)
            pe.wait_ge(tab["ke"], 1)
            pe.wait_ge(tab["vwo"], 1)
            for i in range(8):
                m, half = divmod(i, 2)
                t.matmul(bank[i][:, :], t_qT[:, m, :], t_KE[:, m, 4 * half:4 * half + 4, :],
                         start=True, stop=True).then_inc(tab["s_mm"], 1)
            pe.wait_ge(tab["lo"], 2)
            pe.wait_ge(tab["vone"], 1)
            pe.wait_ge(onehot, 2)

            def slots(n, att, ffn, m):
                for s in range(SLOTS):
                    if att and s < GB:
                        k, hg = divmod(s, GT)
                        if not isinstance(n, int) or n * GB + s > 0:
                            pe.wait_ge(t_added, n * GB + s)
                        oh = OT[:, bass.ds(n * BLK + k * P, P)]
                        t.matmul(b_S[:, :], oh, Sh[:, hg * GW:(hg + 1) * GW], start=True, stop=False)
                        t.matmul(b_S[:, :], oh, Sl[:, hg * GW:(hg + 1) * GW], start=False, stop=True).then_inc(scores, 1)
                    if att and 2 <= s < GB + 2:
                        q = s - 2
                        pe.wait_ge(w_rdy, n * GB + q + 1)
                        if not isinstance(n, int) or n * GB + q > 0:
                            pe.wait_ge(wt_lo, n * GB + q)
                        for h in range(REP):
                            last = t.transpose(b_WT[:, h * P:(h + 1) * P], T[q % 4][:, h * P:(h + 1) * P], ident[:, :])
                        last.then_inc(wt_rdy, 1)
                    if att and 3 <= s < GB + 3:
                        q = s - 3
                        hg = q % GT
                        pe.wait_ge(wt_lo, n * GB + q + 1)
                        if not isinstance(n, int) or n * GB + q > 0:
                            pe.wait_ge(pv_ev, n * GB + q)
                        for h in range(REP):
                            o = b_PV[:, h * PVW:(h + 1) * PVW]
                            t.matmul(o, WTh[q % 2][:, h * P:(h + 1) * P], Va3[:, hg, :], start=True, stop=False)
                            last = t.matmul(o, WTl[q % 2][:, h * P:(h + 1) * P], Va3[:, hg, :], start=False, stop=True)
                        last.then_inc(pv_rdy, 1)
                    for k in range(TPB):
                        tl = n * TPB + k
                        later = not isinstance(n, int) or tl > 0
                        if att and s == H0_SLOT[k]:
                            if later:
                                pe.wait_ge(xt_lo, tl)
                            oh = OT[:, bass.ds(n * BLK + k * P, P)]
                            t.matmul(b_tail[:, :], oh, H0[:, 0:D], start=True, stop=False)
                            t.matmul(b_tail[:, :], oh, H0[:, D:2 * D], start=False, stop=True).then_inc(h0_rdy, 1)
                        if att and s == YT_SLOT[k]:
                            pe.wait_ge(y_rdy, tl + 1)
                            pe.wait_ge(h0_ev, tl + 1)
                            for c in range(DC):
                                last = t.transpose(b_tail[:, c * P:(c + 1) * P], y[:, c * P:(c + 1) * P], ident[:, :])
                            last.then_inc(yt_rdy, 1)
                        if att and s == WO_SLOT[k]:
                            pe.wait_ge(yt_lo, tl + 1)
                            for c in range(DC):
                                yh, yl = (yT[:, i * D + c * P:i * D + (c + 1) * P] for i in (0, 1))
                                t.matmul(b_tail[:, :], yh, Woh[:, c, :], start=c == 0, stop=False)
                                t.matmul(b_tail[:, :], yh, Wol[:, c, :], start=False, stop=False)
                                last = t.matmul(b_tail[:, :], yl, Woh[:, c, :], start=False, stop=c == DC - 1)
                            last.then_inc(wo_rdy, 1)
                        if att and s == XN_SLOT[k]:
                            pe.wait_ge(xn_rdy, tl + 1)
                            for c in range(DC):
                                last = t.transpose(b_tail[:, c * P:(c + 1) * P], xn[:, c * P:(c + 1) * P], ident[:, :])
                            last.then_inc(xt_rdy, 1)
                    if ffn and s < HC:
                        if s == 0:
                            pe.wait_ge(xt_lo, m * TPB + TPB)
                        if s >= 4:
                            pe.wait_ge(g2_rdy, m * HC + s - 3)
                        if s == 1:
                            pe.wait_ge(fin_rdy, m * TPB + TPB)
                        for wh, wl, at in ((Gh, Gl, 0), (Uh, Ul, BLK)):
                            o = b_ffn[s % 4][:, at:at + BLK]
                            for c in range(DC):
                                wch, wcl = (w[:, c, s * P:(s + 1) * P] for w in (wh, wl))
                                t.matmul(o, wch, xTh[:, c, :], start=c == 0, stop=False)
                                t.matmul(o, wch, xTl[:, c, :], start=False, stop=False)
                                last = t.matmul(o, wcl, xTh[:, c, :], start=False, stop=c == DC - 1)
                        last.then_inc(gu_rdy, 1)
                    if ffn and s >= HC:
                        k, q = divmod(s - HC, 4)
                        if s == HC:
                            for c in range(4):
                                i = piece(2, "split", c)
                                pe.wait_ge(stage_used[i % RING], i // RING + 1)
                        if q == 0:
                            pe.wait_ge(g2_rdy, m * HC + HC - 3 + k)
                        if k == 0:
                            pe.wait_ge(gt_lo, m * HC + 4 * q + 4)
                        for j in range(4 * q, 4 * q + 4):
                            o = b_ffn[k][:, :]
                            hh, hl = (w[:, j, k * P:(k + 1) * P] for w in (gth, gtl))
                            t.matmul(o, hh, Dh[:, j, :], start=j == 0, stop=False)
                            t.matmul(o, hh, Dl[:, j, :], start=False, stop=False)
                            last = t.matmul(o, hl, Dh[:, j, :], start=False, stop=j == HC - 1)
                        if q == 3:
                            last.then_inc(dn_rdy, 1)

            slots(0, True, False, 0)
            for w in (0, 1):
                for c in range(4):
                    i = piece(w, "split", c)
                    pe.wait_ge(stage_used[i % RING], i // RING + 1)
            with pe.Fori(1, BLOCKS) as n:
                slots(n, True, True, n - 1)
            slots(0, False, True, BLOCKS - 1)


def kernel(**inputs):
    import numpy as np
    import concourse.bacc as bacc
    from concourse.bass_utils import run_bass_kernel_spmd

    x = np.asarray(inputs["x"])
    lay = {
        "x_row": x.reshape(1, TOK),
        "x_col": x.reshape(TILES, P).T,
        "emb": inputs["L0_tok_emb_table"],
        "norm_weight": np.asarray(inputs["L0_tok_norm_weight"]).reshape(DC, P).T,
        "projT": np.asarray(inputs["L0_tok_proj_weight"]).T,
        "wq": inputs["L0_attn_wq"],
        "wk": inputs["L0_attn_wk"],
        "wv": inputs["L0_attn_wv"],
        "wo": inputs["L0_attn_wo"],
        "w_gateT": np.asarray(inputs["L0_ffn_w_gate"]).T,
        "w_upT": np.asarray(inputs["L0_ffn_w_up"]).T,
        "w_downT": np.asarray(inputs["L0_ffn_w_down"]).T,
    }
    nc = bacc.Bacc("TRN2", target_bir_lowering=False, num_devices=1)
    arrays, args = {}, []
    for name, a in lay.items():
        a = np.ascontiguousarray(a)
        arrays[f"in_{name}"] = a
        args.append(nc.dram_tensor(f"in_{name}", a.shape, mybir.dt.from_np(a.dtype), kind="ExternalInput").ap())
    args.append(nc.dram_tensor("out_rows_dram", (TOK, D), F32, kind="ExternalOutput").ap())
    lm_block(nc, *args)
    r = run_bass_kernel_spmd(nc, [arrays], core_ids=[0])
    return r.results[0]["out_rows_dram"].reshape(B, SEQ, D)
```
